# Optimizing a Trainium2 kernel written in Bass

```python
import numpy as np
import jax
import jax.numpy as jnp

def _softmax(x, axis=-1):
    return jax.nn.softmax(x, axis=axis)

def _gelu(x):
    return jax.nn.gelu(x, approximate=True)

def _silu(x):
    return jax.nn.silu(x)

def _sigmoid(x):
    return jax.nn.sigmoid(x)

def _layernorm(x, axis=-1, eps=1e-05):
    m = jnp.mean(x, axis=axis, keepdims=True)
    v = jnp.var(x, axis=axis, keepdims=True)
    return (x - m) / jnp.sqrt(v + eps)

def _scatter_add(tgt, idx, src, axis=0):
    return tgt.at[idx].add(src)

def _segment_sum(src, seg, n):
    return jax.ops.segment_sum(src, seg, n)
kernel_name = 'mk_adj_preln_d1_adj_r2_7c0a4e'

def setup_inputs(seed: int=0):
    np.random.seed(seed)
    _w = jnp.asarray

    def _rec_inputs():
        import jax
        import jax.numpy as jnp
        _gk = jax.random.key(seed)
        x = -0.0002928 + 1 * jax.random.normal(jax.random.fold_in(_gk, 1), (2048, 256), jnp.float32)
        _a = jax.random.bernoulli(jax.random.fold_in(_gk, 2), 0.00195312, (2048, 2048))
        _a = jnp.logical_or(_a, jnp.eye(2048, dtype=bool))
        _af = _a.astype(jnp.float32)
        _af = _af * jax.random.uniform(jax.random.fold_in(_gk, 3), (2048, 2048), jnp.float32, 0.05, 1000000000.0)
        adj = _af
        return (x, adj)
    x, adj = _rec_inputs()

    def _L0_gnn_setup():
        import jax, jax.numpy as jnp
        import numpy as np
        N_HEADS = 4
        N_HIDDEN = 256
        SLOPE = 0.01
        NEG = -1000000000.0
        key = jax.random.key(seed)
        k1, k2, k3, k4 = jax.random.split(key, 4)
        N, F_IN = (4096, 256)
        h = jax.random.normal(k1, (N, F_IN), dtype=jnp.float32)
        W = jax.random.normal(k2, (F_IN, N_HIDDEN * N_HEADS), dtype=jnp.float32) * 0.05
        a = jax.random.normal(k3, (N_HEADS, 2 * N_HIDDEN, 1), dtype=jnp.float32) * 0.05
        adj_mat = jnp.where(jax.random.uniform(k4, (N, N)) < 0.01, 0.0, NEG).astype(jnp.float32)
        return {'h': h, 'adj_mat': adj_mat, 'W': W, 'a': a}
    _L0_gnn_all = _L0_gnn_setup()
    _L0_gnn_in = {k: v for k, v in _L0_gnn_all.items() if k in ('W', 'a')}
    del _L0_gnn_all
    return {'x': x, 'adj': adj, 'L0_gnn_W': _L0_gnn_in['W'], 'L0_gnn_a': _L0_gnn_in['a']}

def reference(x, adj, L0_gnn_W, L0_gnn_a):
    import jax
    import jax.numpy as jnp

    def _L0_gnn_ref(h, adj_mat, W, a):
        import jax, jax.numpy as jnp
        import numpy as np
        N_HEADS = 4
        N_HIDDEN = 256
        SLOPE = 0.01
        NEG = -1000000000.0
        N = h.shape[0]
        ht = (h @ W).reshape(N, N_HEADS, N_HIDDEN).transpose(1, 0, 2)
        a_src = a[:, :N_HIDDEN, 0]
        a_dst = a[:, N_HIDDEN:, 0]
        src = jnp.einsum('hnd,hd->hn', ht, a_src)
        dst = jnp.einsum('hnd,hd->hn', ht, a_dst)
        e = jax.nn.leaky_relu(src[:, :, None] + dst[:, None, :], SLOPE) + adj_mat[None]
        att = jax.nn.softmax(e, axis=-1)
        h_prime = jnp.einsum('hij,hjd->hid', att, ht)
        return h_prime.mean(axis=0)
    h = jnp.maximum(_layernorm(x, axis=-1), 0.0)
    x = x + _L0_gnn_ref(h, adj, L0_gnn_W, L0_gnn_a)
    return x

_drawn_inputs = setup_inputs


def setup_inputs(seed=0):
    import zlib

    import numpy as np

    out = dict(_drawn_inputs(seed))
    spreads = {}
    factors = {}
    for name, (base, spread) in spreads.items():
        noise = np.random.default_rng([zlib.crc32(name.encode()), seed]).standard_normal(out[name].shape)
        drawn = base * np.exp(spread * noise) if base else spread * noise
        out[name] = jnp.asarray(drawn.astype(out[name].dtype))
    for name, factor in factors.items():
        out[name] = (out[name] * factor).astype(out[name].dtype)
    return out
```

```python
from contextlib import ExitStack

import concourse.bass as bass
from concourse import mybir

ALU = mybir.AluOpType
ACT = mybir.ActivationFunctionType
F32 = mybir.dt.float32
F16 = mybir.dt.float16

P = 128
EPS = 1e-5
FLT_MAX = 3.4028235e38
SLOPE = 0.01
H_SCALE = 2.0 ** 11
W_SCALE = 2.0 ** 14


def gat_layer(nc, x, adj, W, a, out):
    N, F = x.shape
    HEADS, D2, _ = a.shape
    D = D2 // 2
    TILES = N // P
    KC = F // P
    HALF = TILES // 2
    GROUPS = 2 * HEADS
    NH = HEADS * TILES
    LB = 4
    BATCHES = TILES // LB
    DBLK = N // 2 // 512
    MM_PER_GROUP = KC * TILES // GROUPS
    assert HEADS == 4 and KC == 2 and D == F and N == 2048
    HI_ON_DVE = (3, 7)

    ctx = ExitStack()
    with ctx:
        def sb(name, shape, dt):
            return ctx.enter_context(nc.sbuf_tensor(name, shape, dt))

        def sem(name):
            return ctx.enter_context(nc.semaphore(name))

        dst_rows = sb("dst_rows", [P, HEADS, N], F32)
        h_hi = sb("h_hi", [P, TILES, F], F16)
        h_lo = sb("h_lo", [P, TILES, F], F16)
        w_sb = sb("w_sb", [P, KC, HEADS * D], F32)
        src_col = sb("src_col", [P, NH], F32)
        adj_sb = sb("adj_sb", [P, 2, N], F32)
        biased = sb("biased", [P, 2, N], F32)
        e = sb("e", [P, HEADS, N], F32)
        wt = sb("wt", [P, 2, 2, TILES, HEADS * P], F16)
        u_sb = sb("u_sb", [P, KC, HEADS * P], F32)
        neg_max = sb("neg_max", [P, HEADS], F32)
        row_sum = sb("row_sum", [P, 2, HEADS], F32)
        row_inv = sb("row_inv", [P, 2, HEADS], F32)
        x_res = sb("x_res", [P, 2, F], F32)
        o_sb = sb("o_sb", [P, 2, F], F32)
        ident = sb("ident", [P, P], F32)
        mean_var = sb("mean_var", [P, TILES, 2], F32)
        stats = sb("stats", [P, TILES, 6], F32)
        var_eps = sb("var_eps", [P, TILES], F32)
        std = sb("std", [P, TILES], F32)
        rstd = sb("rstd", [P, TILES], F32)
        newton = sb("newton", [P, TILES], F32)
        wa = sb("wa", [P, KC, 2, HEADS], F32)
        wa_rep = biased[:, 1, 0:KC * HEADS * P].rearrange("p (k h m) -> p k h m", k=KC, h=HEADS)
        x_sb = wt[:, 0, 0, :, :].rearrange("p c m -> p (c m)").bitcast(F32).rearrange("p (t f) -> p t f", t=TILES)
        h_sb = wt[:, 0, 1, :, :].rearrange("p c m -> p (c m)").bitcast(F32).rearrange("p (t f) -> p t f", t=TILES)
        a_sb = wt[:, 1, 0, 0:TILES // 2, :].rearrange("p c m -> p (c m)").bitcast(F32).rearrange(
            "p (h s d) -> p h s d", h=HEADS, s=2)
        prod = wt[:, 1, 1, :, :].bitcast(F32)
        hT = e[:, 2:4, :]

        tp = ctx.enter_context(nc.psum_tensor("tp", [P, 2, HALF * P], F32))
        u_ps = ctx.enter_context(nc.psum_tensor("u_ps", [P, KC, HEADS * P], F32))
        f_ps = ctx.enter_context(nc.psum_tensor("f_ps", [P, HEADS, D], F32))
        pair = [u_ps[:, :, :].rearrange("p k m -> p (k m)"), f_ps[:, :, :].rearrange("p h d -> p (h d)")]
        src_ps = tp[:, 0, 0:NH]
        

        x_batch_in = [sem(f"x_batch_in{k}") for k in range(BATCHES)]
        w_in = sem("w_in")
        a_in = sem("a_in")
        adj_in = [sem(f"adj_in{u}") for u in range(2)]
        x_res_in = [sem(f"x_res_in{u}") for u in range(2)]
        out_written = [sem(f"out_written{u}") for u in range(2)]
        ident_zero = sem("ident_zero")
        ident_ready = sem("ident_ready")
        ln_step = sem("ln_step")
        var_ready = sem("var_ready")
        std_ready = sem("std_ready")
        z_ready = sem("z_ready")
        h_ready = sem("h_ready")
        hT_in_psum = sem("hT_in_psum")
        hT_ready = sem("hT_ready")
        h_split = sem("h_split")
        wa_done = sem("wa_done")
        wa_ready = sem("wa_ready")
        src_in_psum = sem("src_in_psum")
        src_ready = sem("src_ready")
        dst_in_psum = sem("dst_in_psum")
        dst_ready = sem("dst_ready")
        relu_done = sem("relu_done")
        biased_done = sem("biased_done")
        max_done = sem("max_done")
        exp_done = sem("exp_done")
        transposed = sem("transposed")
        hi_by_act = sem("hi_by_act")
        hi_by_dve = sem("hi_by_dve")
        lo_done = sem("lo_done")
        u_done = sem("u_done")
        u_copied = sem("u_copied")
        final_done = sem("final_done")
        inv_step = sem("inv_step")
        inv_done = sem("inv_done")
        acc_step = sem("acc_step")
        acc_done = sem("acc_done")

        block = ctx.enter_context(nc.Block())

        def wait(eng, s, count):
            if not (isinstance(count, int) and count <= 0):
                eng.wait_ge(s, count)

        x_t = x.rearrange("(t p) f -> p t f", p=P)

        @block.sync
        def _(sp):
            for k in range(BATCHES):
                sp.dma_start(x_sb[:, LB * k:LB * (k + 1), :], x_t[:, LB * k:LB * (k + 1), :]).then_inc(
                    x_batch_in[k], 16)

            def load_tile(t, u):
                wait(sp, biased_done, HEADS * (t - 1))
                sp.dma_start(adj_sb[:, u, :], adj[bass.ts(t, P), :]).then_inc(adj_in[u], 16)
                wait(sp, acc_done, t - 1)
                sp.dma_start(x_res[:, u, :], x[bass.ts(t, P), :]).then_inc(x_res_in[u], 16)

            def store_tile(t, u):
                sp.wait_ge(acc_done, t + 1)
                sp.dma_start(out[bass.ts(t, P), :], o_sb[:, u, :]).then_inc(out_written[u], 16)

            load_tile(0, 0)
            load_tile(1, 1)
            with sp.Fori(1, TILES // 2) as p:
                for u in range(2):
                    sp.wait_ge(biased_done, HEADS * (2 * p + u - 1))
                    sp.dma_start(adj_sb[:, u, :], adj[bass.ts(2 * p + u, P), :]).then_inc(adj_in[u], 16)
                    sp.wait_ge(acc_done, 2 * p + u - 1)
                    sp.dma_start(out[bass.ts(2 * p + u - 2, P), :], o_sb[:, u, :]).then_inc(out_written[u], 16)
                    sp.dma_start(x_res[:, u, :], x[bass.ts(2 * p + u, P), :]).then_inc(x_res_in[u], 16)
            store_tile(TILES - 2, 0)
            store_tile(TILES - 1, 1)
            for u in range(2):
                sp.wait_ge(out_written[u], 16 * (TILES // 2))

        @block.gpsimd
        def _(pool):
            nc.gpsimd.memset(ident[:, :], 0.0).then_inc(ident_zero, 1)
            pool.wait_ge(ident_zero, 1)
            nc.gpsimd.affine_select(out=ident[:, :], in_=ident[:, :], compare_op=ALU.not_equal, fill=1.0,
                                    base=0, pattern=[[-1, P]], channel_multiplier=1).then_inc(ident_ready, 1)

            def add_bias(n, h, u, p):
                if h == 0:
                    pool.wait_ge(adj_in[u], 16 * (p + 1))
                wait(pool, max_done, n - 1)
                nc.gpsimd.tensor_tensor(biased[:, h % 2, :], adj_sb[:, u, :], dst_rows[:, h, :],
                                        ALU.add).then_inc(biased_done, 1)

            for n in range(2 * HEADS):
                if n < HEADS:
                    pool.wait_ge(dst_ready, 2 * n + 2)
                if n == 1:
                    pool.wait_ge(dst_ready, 2 * HEADS)
                add_bias(n, n % HEADS, n // HEADS, 0)
            with pool.Fori(1, TILES // 2) as p:
                for u in range(2):
                    for h in range(HEADS):
                        add_bias(HEADS * (2 * p + u) + h, h, u, p)

        @block.tensor
        def _(pe):
            def transpose_group(t, g):
                h, half = g // 2, g % 2
                pe.wait_ge(exp_done, HEADS * t + h + 1)
                wait(pe, lo_done, GROUPS * t + g - 1)
                for b in range(HALF):
                    c = HALF * half + b
                    last = pe.transpose(tp[:, g % 2, b * P:(b + 1) * P], e[:, h, c * P:(c + 1) * P], ident[:, :])
                last.then_inc(transposed, 1)

            def weighted_sum(t, u, g):
                f, quarter = g // (GROUPS // KC), g % (GROUPS // KC)
                if g == 0:
                    pe.wait_ge(lo_done, GROUPS * t + GROUPS - 1)
                if g == 2:
                    pe.wait_ge(lo_done, GROUPS * t + GROUPS)
                if quarter == 0:
                    wait(pe, u_copied, KC * (t - 1) + f + 1)
                for c in range(MM_PER_GROUP * quarter, MM_PER_GROUP * (quarter + 1)):
                    hi = h_hi[:, c, f * P:(f + 1) * P]
                    lo = h_lo[:, c, f * P:(f + 1) * P]
                    pe.matmul(u_ps[:, f, :], hi, wt[:, u, 0, c, :], start=(c == 0), stop=False)
                    pe.matmul(u_ps[:, f, :], hi, wt[:, u, 1, c, :], start=False, stop=False)
                    last = pe.matmul(u_ps[:, f, :], lo, wt[:, u, 0, c, :], start=False, stop=(c == TILES - 1))
                if quarter == GROUPS // KC - 1:
                    last.then_inc(u_done, 1)

            def final_products(t):
                pe.wait_ge(u_copied, KC * (t + 1))
                wait(pe, acc_done, t)
                for h in range(HEADS):
                    for k in range(KC):
                        last = pe.matmul(f_ps[:, h, :], u_sb[:, k, h * P:(h + 1) * P], w_sb[:, k, h * D:(h + 1) * D],
                                         start=(k == 0), stop=(k == KC - 1))
                last.then_inc(final_done, 1)

            def step(t, u, transposes=True, sums=True, finals=True):
                for g in range(GROUPS):
                    if transposes:
                        transpose_group(t, g)
                    if sums:
                        weighted_sum(t - 1, 1 - u, g)
                    if finals and g == 1:
                        final_products(t - 2)

            pe.wait_ge(ident_ready, 1)
            for k in range(BATCHES):
                pe.wait_ge(h_ready, k + 1)
                wait(pe, hT_ready, k - 1)
                for f in range(KC):
                    for b in range(LB):
                        at = (f * LB + b) * P
                        last = pe.transpose(pair[k % 2][:, at:at + P], h_sb[:, LB * k + b, f * P:(f + 1) * P],
                                            ident[:, :])
                last.then_inc(hT_in_psum, 1)
            pe.wait_ge(hT_ready, BATCHES)
            pe.wait_ge(wa_ready, 1)
            for t in range(TILES):
                for k in range(KC):
                    last = pe.matmul(src_ps[:, HEADS * t:HEADS * (t + 1)], hT[:, k, t * P:(t + 1) * P],
                                     wa[:, k, 0, :], start=(k == 0), stop=(k == KC - 1))
            last.then_inc(src_in_psum, 1)
            for r in range(2 * HEADS):
                h, half = r // 2, r % 2
                wait(pe, dst_ready, r - 1)
                for b in range(DBLK):
                    j = (half * DBLK + b) * 512
                    for k in range(KC):
                        last = pe.matmul(pair[r % 2][:, b * 512:(b + 1) * 512], wa_rep[:, k, h, :],
                                         hT[:, k, j:j + 512], start=(k == 0), stop=(k == KC - 1))
                last.then_inc(dst_in_psum, 1)
            pe.wait_ge(h_split, 1)
            pe.wait_ge(dst_ready, 2 * HEADS)
            step(0, 0, sums=False, finals=False)
            step(1, 1, finals=False)
            with pe.Fori(1, TILES // 2) as p:
                for u in range(2):
                    step(2 * p + u, u)
            step(TILES, 0, transposes=False)
            step(TILES + 1, 1, transposes=False, sums=False)

        @block.scalar
        def _(act):
            act.dma_start(w_sb[:, :, :], W.rearrange("(k p) n -> p k n", p=P)).then_inc(w_in, 16)
            act.dma_start(a_sb.rearrange("p h s d -> p (h s d)"), a.rearrange("h d o -> o (h d)").to_broadcast(
                [P, HEADS * 2 * D])).then_inc(a_in, 16)
            act.wait_ge(var_ready, 1)
            nc.scalar.activation(std[:, :], var_eps[:, :], ACT.Sqrt).then_inc(std_ready, 1)
            for k in range(BATCHES):
                act.wait_ge(z_ready, k + 1)
                nc.scalar.activation(h_sb[:, LB * k:LB * (k + 1), :], x_sb[:, LB * k:LB * (k + 1), :],
                                     ACT.Relu).then_inc(h_ready, 1)
                act.wait_ge(hT_in_psum, k + 1)
                nc.scalar.copy(hT[:, :, 512 * k:512 * (k + 1)],
                               pair[k % 2].rearrange("p (f j) -> p f j", f=KC)).then_inc(hT_ready, 1)

            def relu(n, h):
                if isinstance(n, int) and n < HEADS:
                    act.wait_ge(dst_ready, 2 * h + 2)
                    if n == 0:
                        act.wait_ge(src_ready, 1)
                    if n == 2:
                        act.wait_ge(dst_ready, 2 * HEADS)
                wait(act, transposed, 2 * (n - HEADS) + 2)
                nc.scalar.activation(e[:, h, :], dst_rows[:, h, :], ACT.Relu, bias=src_col[:, bass.ds(n, 1)],
                                     scale=(1 - SLOPE) / SLOPE).then_inc(relu_done, 1)

            def exp(n, h, u, t):
                act.wait_ge(max_done, n + 1)
                if h == 0:
                    wait(act, inv_done, t)
                nc.scalar.activation(e[:, h, :], e[:, h, :], ACT.Exp, bias=neg_max[:, h:h + 1], scale=-1.0,
                                     accum_out=row_sum[:, u, h:h + 1]).then_inc(exp_done, 1)

            def split_hi(t, u, g):
                h, half = g // 2, g % 2
                act.wait_ge(transposed, GROUPS * t + g + 1)
                if g == 0:
                    wait(act, u_done, KC * (t - 1))
                nc.scalar.activation(wt[:, u, 0, HALF * half:HALF * (half + 1), h * P:(h + 1) * P],
                                     tp[:, g % 2, :].rearrange("p (c i) -> p c i", c=HALF),
                                     ACT.Copy, scale=W_SCALE).then_inc(hi_by_act, 1)

            def copy_u(t, f):
                act.wait_ge(u_done, KC * t + f + 1)
                wait(act, final_done, t)
                nc.scalar.copy(u_sb[:, f, :], u_ps[:, f, :]).then_inc(u_copied, 1)

            def slot(t, u, h):
                if 2 * h not in HI_ON_DVE:
                    split_hi(t, u, 2 * h)
                static = isinstance(t, int)
                if h == 0 and not (static and t < 2):
                    copy_u(t - 2, 1)
                if h == 2 and not (static and t < 1):
                    copy_u(t - 1, 0)
                h1, h3 = (h + 1) % HEADS, (h + 3) % HEADS
                n = HEADS * t + h
                if not (static and n + 1 >= NH):
                    exp(n + 1, h1, u if h1 else 1 - u, t)
                if 2 * h + 1 not in HI_ON_DVE:
                    split_hi(t, u, 2 * h + 1)
                if not (static and n + 3 >= NH):
                    relu(n + 3, h3)

            relu(0, 0)
            relu(1, 1)
            exp(0, 0, 0, 0)
            relu(2, 2)
            for t in range(2):
                for h in range(HEADS):
                    slot(t, t, h)
            with act.Fori(1, TILES // 2 - 1) as p:
                for u in range(2):
                    for h in range(HEADS):
                        slot(2 * p + u, u, h)
            for t in range(TILES - 2, TILES):
                for h in range(HEADS):
                    slot(t, t % 2, h)
            copy_u(TILES - 2, 1)
            copy_u(TILES - 1, 0)
            copy_u(TILES - 1, 1)

        @block.vector
        def _(dve):
            steps = [0]

            def link(ins):
                steps[0] += 1
                ins.then_inc(ln_step, 1)
                dve.wait_ge(ln_step, steps[0])

            for k in range(BATCHES):
                dve.wait_ge(x_batch_in[k], 16)
                for t in range(LB * k, LB * (k + 1)):
                    last = nc.vector.bn_stats(stats[:, t, :], x_sb[:, t, :])
            link(last)
            for t in range(TILES):
                last = nc.vector.bn_aggr(mean_var[:, t, :], stats[:, t, :])
            link(last)
            nc.vector.tensor_scalar(var_eps[:, :], mean_var[:, :, 1], EPS, None, ALU.add).then_inc(var_ready, 1)
            dve.wait_ge(w_in, 16)
            dve.wait_ge(a_in, 16)
            for k in range(KC):
                for s in range(2):
                    for h in range(HEADS):
                        last = nc.vector.tensor_tensor_reduce(
                            prod[:, (2 * k + s) * HEADS + h, :], w_sb[:, k, h * D:(h + 1) * D], a_sb[:, h, s, :], 1.0, 0.0, ALU.mult, ALU.add,
                            wa[:, k, s, h:h + 1])
            last.then_inc(wa_done, 1)
            dve.wait_ge(std_ready, 1)
            link(nc.vector.reciprocal(rstd[:, :], std[:, :]))
            link(nc.vector.tensor_tensor(newton[:, :], rstd[:, :], rstd[:, :], ALU.mult))
            link(nc.vector.tensor_tensor(newton[:, :], newton[:, :], var_eps[:, :], ALU.mult))
            link(nc.vector.tensor_scalar(newton[:, :], newton[:, :], -0.5, 1.5, ALU.mult, ALU.add))
            link(nc.vector.tensor_tensor(rstd[:, :], rstd[:, :], newton[:, :], ALU.mult))
            for k in range(BATCHES):
                for t in range(LB * k, LB * (k + 1)):
                    last = nc.vector.tensor_scalar(x_sb[:, t, :], x_sb[:, t, :], mean_var[:, t, 0:1],
                                                   rstd[:, t:t + 1], ALU.subtract, ALU.mult)
                last.then_inc(z_ready, 1)
            dve.wait_ge(wa_done, 1)
            nc.vector.tensor_copy(wa_rep[:, :, :, :].rearrange("p k h m -> p (k h) m") if False else
                                  wa_rep[:, :, :, :],
                                  wa[:, :, 1, :].unsqueeze(3).to_broadcast([P, KC, HEADS, P])).then_inc(wa_ready, 1)

            def copy_dst(r):
                h, half = r // 2, r % 2
                dve.wait_ge(dst_in_psum, r + 1)
                nc.vector.tensor_scalar(dst_rows[:, h, half * (N // 2):(half + 1) * (N // 2)], pair[r % 2], SLOPE,
                                        None, ALU.mult).then_inc(dst_ready, 1)

            def wait_scores(n):
                dve.wait_ge(relu_done, n + 1)
                dve.wait_ge(biased_done, n + 1)
                wait(dve, exp_done, n - HEADS + 1)

            def scores(h):
                nc.vector.tensor_tensor_reduce(e[:, h, :], e[:, h, :], biased[:, h % 2, :], -1.0, FLT_MAX, ALU.add,
                                               ALU.min, neg_max[:, h:h + 1]).then_inc(max_done, 1)

            dve.wait_ge(src_in_psum, 1)
            nc.vector.tensor_scalar(src_col[:, :], src_ps, 1 - SLOPE, None, ALU.mult).then_inc(src_ready, 1)
            copy_dst(0)
            copy_dst(1)
            dve.wait_ge(h_ready, BATCHES)
            link(nc.vector.tensor_scalar(h_hi[:, :, :], h_sb[:, :, :], H_SCALE, None, ALU.mult))
            copy_dst(2)
            copy_dst(3)
            nc.vector.scalar_tensor_tensor(
                h_lo[:, :, :].rearrange("p t f -> p (t f)"), h_sb[:, :, :].rearrange("p t f -> p (t f)"), H_SCALE,
                h_hi[:, :, :].rearrange("p t f -> p (t f)"), ALU.mult, ALU.subtract).then_inc(h_split, 1)
            wait_scores(0)
            scores(0)
            copy_dst(4)
            copy_dst(5)
            copy_dst(6)
            copy_dst(7)
            wait_scores(1)
            scores(1)

            def act_his(g):
                return sum(1 for k in range(g + 1) if k not in HI_ON_DVE)

            def split(t, u, g):
                h, half = g // 2, g % 2
                hi = wt[:, u, 0, HALF * half:HALF * (half + 1), h * P:(h + 1) * P]
                lo = wt[:, u, 1, HALF * half:HALF * (half + 1), h * P:(h + 1) * P]
                group = tp[:, g % 2, :].rearrange("p (c i) -> p c i", c=HALF)
                if g == 0:
                    wait(dve, u_done, KC * (t - 1))
                if g in HI_ON_DVE:
                    dve.wait_ge(transposed, GROUPS * t + g + 1)
                    nc.vector.tensor_scalar(hi, group, W_SCALE, None, ALU.mult).then_inc(hi_by_dve, 1)
                    dve.wait_ge(hi_by_dve, len(HI_ON_DVE) * t + HI_ON_DVE.index(g) + 1)
                else:
                    dve.wait_ge(hi_by_act, act_his(GROUPS - 1) * t + act_his(g))
                nc.vector.scalar_tensor_tensor(lo, group, W_SCALE, hi, ALU.mult, ALU.subtract).then_inc(lo_done, 1)

            def invert_sums(t, u):
                dve.wait_ge(exp_done, HEADS * (t + 1))
                wait(dve, acc_done, t - 1)
                nc.vector.tensor_scalar(row_inv[:, u, :], row_sum[:, u, :], HEADS * H_SCALE * W_SCALE, None,
                                        ALU.mult).then_inc(inv_step, 1)
                dve.wait_ge(inv_step, t + 1)
                nc.vector.reciprocal(row_inv[:, u, :], row_inv[:, u, :]).then_inc(inv_done, 1)

            def output(t, u, p):
                dve.wait_ge(final_done, t + 1)
                dve.wait_ge(inv_done, t + 1)
                dve.wait_ge(x_res_in[u], 16 * (p + 1))
                wait(dve, out_written[u], 16 * p)
                for h in range(HEADS):
                    last = nc.vector.scalar_tensor_tensor(
                        o_sb[:, u, :], f_ps[:, h, :], row_inv[:, u, h:h + 1], x_res[:, u, :] if h == 0 else o_sb[:, u, :],
                        ALU.mult, ALU.add)
                    if h < HEADS - 1:
                        last.then_inc(acc_step, 1)
                        dve.wait_ge(acc_step, (HEADS - 1) * t + h + 1)
                last.then_inc(acc_done, 1)

            def slot(t, u, p, h):
                static = isinstance(t, int)
                n = HEADS * t + h
                more = not (static and n + 2 >= NH)
                h2 = (h + 2) % HEADS
                if more:
                    wait_scores(n + 2)
                split(t, u, 2 * h)
                if more:
                    scores(h2)
                split(t, u, 2 * h + 1)
                if h == 0 and not (static and t < 1):
                    invert_sums(t - 1, 1 - u)
                if h == 1 and not (static and t < 2):
                    output(t - 2, u, p - 1)

            for t in range(2):
                for h in range(HEADS):
                    slot(t, t, 0, h)
            with dve.Fori(1, TILES // 2 - 1) as p:
                for u in range(2):
                    for h in range(HEADS):
                        slot(2 * p + u, u, p, h)
            for t in range(TILES - 2, TILES):
                for h in range(HEADS):
                    slot(t, t % 2, t // 2, h)
            invert_sums(TILES - 1, 1)
            output(TILES - 2, 0, TILES // 2 - 1)
            output(TILES - 1, 1, TILES // 2 - 1)


_INS = ['x', 'adj', 'L0_gnn_W', 'L0_gnn_a']


def kernel(**inputs):
    import numpy as _np
    import concourse.bacc as _bacc
    from concourse import mybir as _mybir
    from concourse.bass_utils import run_bass_kernel_spmd as _run

    nc = _bacc.Bacc("TRN2", target_bir_lowering=False, num_devices=1)
    arrays, args = {}, []
    for name in _INS:
        arr = _np.ascontiguousarray(inputs[name])
        arrays[f"in_{name}_dram"] = arr
        args.append(nc.dram_tensor(f"in_{name}_dram", arr.shape, _mybir.dt.from_np(arr.dtype), kind="ExternalInput").ap())
    out = nc.dram_tensor("out_dram", inputs['x'].shape, _mybir.dt.float32, kind="ExternalOutput").ap()
    gat_layer(nc, *args, out)
    r = _run(nc, [arrays], core_ids=[0])
    return r.results[0]["out_dram"]
```

```python
from contextlib import ExitStack

import concourse.bass as bass
from concourse import mybir

ALU = mybir.AluOpType
ACT = mybir.ActivationFunctionType
F32 = mybir.dt.float32
F16 = mybir.dt.float16

P = 128
EPS = 1e-5
FLT_MAX = 3.4028235e38
SLOPE = 0.01
H_SCALE = 2.0 ** 11
W_SCALE = 2.0 ** 14


def gat_layer(nc, x, adj, W, a, out):
    N, F = x.shape
    HEADS, D2, _ = a.shape
    D = D2 // 2
    TILES = N // P
    KC = F // P
    HALF = TILES // 2
    GROUPS = 2 * HEADS
    NH = HEADS * TILES
    LB = 4
    BATCHES = TILES // LB
    DBLK = N // 2 // 512
    MM_PER_GROUP = KC * TILES // GROUPS
    assert HEADS == 4 and KC == 2 and D == F and N == 2048
    HI_ON_DVE = (3, 7)

    ctx = ExitStack()
    with ctx:
        def sb(name, shape, dt):
            return ctx.enter_context(nc.sbuf_tensor(name, shape, dt))

        def sem(name):
            return ctx.enter_context(nc.semaphore(name))

        dst_rows = sb("dst_rows", [P, HEADS, N], F32)
        h_hi = sb("h_hi", [P, TILES, F], F16)
        h_lo = sb("h_lo", [P, TILES, F], F16)
        w_sb = sb("w_sb", [P, KC, HEADS * D], F32)
        src_col = sb("src_col", [P, NH], F32)
        adj_sb = sb("adj_sb", [P, 2, N], F32)
        biased = sb("biased", [P, 2, N], F32)
        e = sb("e", [P, HEADS, N], F32)
        wt = sb("wt", [P, 2, 2, TILES, HEADS * P], F16)
        u_sb = sb("u_sb", [P, KC, HEADS * P], F32)
        neg_max = sb("neg_max", [P, HEADS], F32)
        row_sum = sb("row_sum", [P, 2, HEADS], F32)
        row_inv = sb("row_inv", [P, 2, HEADS], F32)
        x_res = sb("x_res", [P, 2, F], F32)
        o_sb = sb("o_sb", [P, 2, F], F32)
        ident = sb("ident", [P, P], F32)
        mean_var = sb("mean_var", [P, TILES, 2], F32)
        stats = sb("stats", [P, TILES, 6], F32)
        var_eps = sb("var_eps", [P, TILES], F32)
        std = sb("std", [P, TILES], F32)
        rstd = sb("rstd", [P, TILES], F32)
        newton = sb("newton", [P, TILES], F32)
        shift = sb("shift", [P, TILES], F32)
        wa = sb("wa", [P, KC, 2 * HEADS], F32)
        rows = sb("rows", [2 * HEADS, N], F32)
        pick = sb("pick", [2 * HEADS, HEADS, P], F32)
        x_sb = wt[:, 0, 0, :, :].rearrange("p c m -> p (c m)").bitcast(F32).rearrange("p (t f) -> p t f", t=TILES)
        h_sb = wt[:, 0, 1, :, :].rearrange("p c m -> p (c m)").bitcast(F32).rearrange("p (t f) -> p t f", t=TILES)
        a_sb = wt[:, 1, 0, 0:TILES // 2, :].rearrange("p c m -> p (c m)").bitcast(F32).rearrange(
            "p (h s d) -> p h s d", h=HEADS, s=2)
        prod = wt[:, 1, 1, :, :].bitcast(F32)
        hT = e[:, 2:4, :]

        tp = ctx.enter_context(nc.psum_tensor("tp", [P, 2, HALF * P], F32))
        u_ps = ctx.enter_context(nc.psum_tensor("u_ps", [P, KC, HEADS * P], F32))
        f_ps = ctx.enter_context(nc.psum_tensor("f_ps", [P, HEADS, D], F32))
        pair = [u_ps[:, :, :].rearrange("p k m -> p (k m)"), f_ps[:, :, :].rearrange("p h d -> p (h d)")]
        src_ps = tp[:, 0, 0:TILES * 2 * HEADS].rearrange("p (t c) -> p t c", t=TILES)
        rows_ps = tp[:, :, :].rearrange("p a m -> p (a m)")[0:2 * HEADS, :]
        

        x_batch_in = [sem(f"x_batch_in{k}") for k in range(BATCHES)]
        w_in = sem("w_in")
        a_in = sem("a_in")
        adj_in = [sem(f"adj_in{u}") for u in range(2)]
        x_res_in = [sem(f"x_res_in{u}") for u in range(2)]
        out_written = [sem(f"out_written{u}") for u in range(2)]
        ident_zero = sem("ident_zero")
        ident_ready = sem("ident_ready")
        ln_step = sem("ln_step")
        var_ready = sem("var_ready")
        std_ready = sem("std_ready")
        norm_ready = sem("norm_ready")
        h_ready = sem("h_ready")
        hT_in_psum = sem("hT_in_psum")
        hT_ready = sem("hT_ready")
        h_split = sem("h_split")
        h_hi_ready = sem("h_hi_ready")
        wa_ready = sem("wa_ready")
        pick_ready = sem("pick_ready")
        rows_in_psum = sem("rows_in_psum")
        rows_ready = sem("rows_ready")
        src_in_psum = sem("src_in_psum")
        src_ready = sem("src_ready")
        dst_in_psum = sem("dst_in_psum")
        dst_ready = sem("dst_ready")
        relu_done = sem("relu_done")
        biased_done = sem("biased_done")
        max_done = sem("max_done")
        exp_done = sem("exp_done")
        transposed = sem("transposed")
        hi_by_act = sem("hi_by_act")
        hi_by_dve = sem("hi_by_dve")
        lo_done = sem("lo_done")
        u_done = sem("u_done")
        u_copied = sem("u_copied")
        final_done = sem("final_done")
        inv_step = sem("inv_step")
        inv_done = sem("inv_done")
        acc_step = sem("acc_step")
        acc_done = sem("acc_done")

        block = ctx.enter_context(nc.Block())

        def wait(eng, s, count):
            if not (isinstance(count, int) and count <= 0):
                eng.wait_ge(s, count)

        x_t = x.rearrange("(t p) f -> p t f", p=P)

        @block.sync
        def _(sp):
            for k in range(BATCHES):
                sp.dma_start(x_sb[:, LB * k:LB * (k + 1), :], x_t[:, LB * k:LB * (k + 1), :]).then_inc(
                    x_batch_in[k], 16)

            sp.dma_start(a_sb.rearrange("p h s d -> p (h s d)"), a.rearrange("h d o -> o (h d)").to_broadcast(
                [P, HEADS * 2 * D])).then_inc(a_in, 16)

            def load_adj(t, u):
                wait(sp, biased_done, HEADS * (t - 1))
                sp.dma_start(adj_sb[:, u, :], adj[bass.ts(t, P), :]).then_inc(adj_in[u], 16)

            def load_x(t, u):
                sp.dma_start(x_res[:, u, :], x[bass.ts(t, P), :]).then_inc(x_res_in[u], 16)

            def store(t, u):
                sp.wait_ge(acc_done, t + 1)
                sp.dma_start(out[bass.ts(t, P), :], o_sb[:, u, :]).then_inc(out_written[u], 16)

            for t in range(2):
                load_adj(t, t)
                load_x(t, t)
            for t in range(2, 4):
                load_adj(t, t % 2)
            with sp.Fori(1, TILES // 2 - 1) as p:
                for u in range(2):
                    store(2 * p + u - 2, u)
                    load_x(2 * p + u, u)
                    load_adj(2 * p + u + 2, u)
            for t in range(TILES - 2, TILES):
                store(t - 2, t % 2)
                load_x(t, t % 2)
            for t in range(TILES - 2, TILES):
                store(t, t % 2)
            for u in range(2):
                sp.wait_ge(out_written[u], 16 * (TILES // 2))

        @block.gpsimd
        def _(pool):
            nc.gpsimd.memset(ident[:, :], 0.0).then_inc(ident_zero, 1)
            pool.wait_ge(ident_zero, 1)
            nc.gpsimd.affine_select(out=ident[:, :], in_=ident[:, :], compare_op=ALU.not_equal, fill=1.0,
                                    base=0, pattern=[[-1, P]], channel_multiplier=1).then_inc(ident_ready, 1)

            pool.wait_ge(ident_ready, 1)
            nc.gpsimd.tensor_copy(pick[:, :, :], ident[0:2 * HEADS, HEADS:2 * HEADS].unsqueeze(2).to_broadcast(
                [2 * HEADS, HEADS, P])).then_inc(pick_ready, 1)
            for k in range(BATCHES):
                batch = slice(LB * k, LB * (k + 1))
                pool.wait_ge(h_ready, k + 1)
                nc.gpsimd.tensor_copy(h_hi[:, batch, :], h_sb[:, batch, :]).then_inc(h_hi_ready, 1)
                pool.wait_ge(h_hi_ready, k + 1)
                nc.gpsimd.tensor_tensor(h_lo[:, batch, :], h_sb[:, batch, :], h_hi[:, batch, :],
                                        ALU.subtract).then_inc(h_split, 1)

            def add_bias(n, h, u, p):
                if h == 0:
                    pool.wait_ge(adj_in[u], 16 * (p + 1))
                wait(pool, max_done, n - 1)
                nc.gpsimd.tensor_tensor(biased[:, h % 2, :], adj_sb[:, u, :], dst_rows[:, h, :],
                                        ALU.add).then_inc(biased_done, 1)

            for n in range(2 * HEADS):
                if n < HEADS:
                    pool.wait_ge(dst_ready, 2 * n + 2)
                add_bias(n, n % HEADS, n // HEADS, 0)
            with pool.Fori(1, TILES // 2) as p:
                for u in range(2):
                    for h in range(HEADS):
                        add_bias(HEADS * (2 * p + u) + h, h, u, p)

        @block.tensor
        def _(pe):
            def transpose_group(t, g):
                h, half = g // 2, g % 2
                pe.wait_ge(exp_done, HEADS * t + h + 1)
                wait(pe, lo_done, GROUPS * t + g - 1)
                for b in range(HALF):
                    c = HALF * half + b
                    last = pe.transpose(tp[:, g % 2, b * P:(b + 1) * P], e[:, h, c * P:(c + 1) * P], ident[:, :])
                last.then_inc(transposed, 1)

            def weighted_sum(t, u, g):
                f, quarter = g // (GROUPS // KC), g % (GROUPS // KC)
                if g == 0:
                    pe.wait_ge(lo_done, GROUPS * t + GROUPS - 1)
                if g == 2:
                    pe.wait_ge(lo_done, GROUPS * t + GROUPS)
                if quarter == 0:
                    wait(pe, u_copied, KC * (t - 1) + f + 1)
                for c in range(MM_PER_GROUP * quarter, MM_PER_GROUP * (quarter + 1)):
                    hi = h_hi[:, c, f * P:(f + 1) * P]
                    lo = h_lo[:, c, f * P:(f + 1) * P]
                    pe.matmul(u_ps[:, f, :], hi, wt[:, u, 0, c, :], start=(c == 0), stop=False)
                    pe.matmul(u_ps[:, f, :], hi, wt[:, u, 1, c, :], start=False, stop=False)
                    last = pe.matmul(u_ps[:, f, :], lo, wt[:, u, 0, c, :], start=False, stop=(c == TILES - 1))
                if quarter == GROUPS // KC - 1:
                    last.then_inc(u_done, 1)

            def final_products(t):
                pe.wait_ge(u_copied, KC * (t + 1))
                wait(pe, acc_done, t)
                for h in range(HEADS):
                    for k in range(KC):
                        last = pe.matmul(f_ps[:, h, :], u_sb[:, k, h * P:(h + 1) * P], w_sb[:, k, h * D:(h + 1) * D],
                                         start=(k == 0), stop=(k == KC - 1))
                last.then_inc(final_done, 1)

            def step(t, u, transposes=True, sums=True, finals=True):
                for g in range(GROUPS):
                    if transposes:
                        transpose_group(t, g)
                    if sums:
                        weighted_sum(t - 1, 1 - u, g)
                    if finals and g == 1:
                        final_products(t - 2)

            pe.wait_ge(ident_ready, 1)
            for k in range(BATCHES):
                pe.wait_ge(h_ready, k + 1)
                wait(pe, hT_ready, k - 1)
                for f in range(KC):
                    for b in range(LB):
                        at = (f * LB + b) * P
                        last = pe.transpose(pair[k % 2][:, at:at + P], h_sb[:, LB * k + b, f * P:(f + 1) * P],
                                            ident[:, :])
                last.then_inc(hT_in_psum, 1)
            pe.wait_ge(wa_ready, 1)
            for k in range(BATCHES):
                pe.wait_ge(hT_ready, k + 1)
                for f in range(KC):
                    last = pe.matmul(rows_ps[:, 512 * k:512 * (k + 1)], wa[:, f, :],
                                     hT[:, f, 512 * k:512 * (k + 1)], start=(f == 0), stop=(f == KC - 1))
                last.then_inc(rows_in_psum, 1)

            def spread_dst(q):
                h, half = q // 2, q % 2
                wait(pe, dst_ready, q - 1)
                for b in range(DBLK):
                    j = (half * DBLK + b) * 512
                    last = pe.matmul(pair[q % 2][:, b * 512:(b + 1) * 512], pick[:, h, :], rows[:, j:j + 512],
                                     start=True, stop=True)
                last.then_inc(dst_in_psum, 1)

            pe.wait_ge(pick_ready, 1)
            pe.wait_ge(rows_ready, BATCHES // 2)
            spread_dst(0)
            pe.wait_ge(rows_ready, BATCHES)
            spread_dst(1)
            for t in range(TILES):
                last = pe.transpose(src_ps[:, t, :], rows[:, t * P:(t + 1) * P], ident[0:2 * HEADS, 0:2 * HEADS])
            last.then_inc(src_in_psum, 1)
            for q in range(2, 2 * HEADS):
                spread_dst(q)
            pe.wait_ge(h_split, BATCHES)
            pe.wait_ge(dst_ready, 2 * HEADS)
            step(0, 0, sums=False, finals=False)
            step(1, 1, finals=False)
            with pe.Fori(1, TILES // 2) as p:
                for u in range(2):
                    step(2 * p + u, u)
            step(TILES, 0, transposes=False)
            step(TILES + 1, 1, transposes=False, sums=False)

        @block.scalar
        def _(act):
            act.dma_start(w_sb[:, :, :], W.rearrange("(k p) n -> p k n", p=P)).then_inc(w_in, 16)
            def root(k):
                act.wait_ge(var_ready, k + 1)
                nc.scalar.activation(std[:, LB * k:LB * (k + 1)], var_eps[:, LB * k:LB * (k + 1)],
                                     ACT.Sqrt).then_inc(std_ready, 1)

            def normalise(k):
                act.wait_ge(norm_ready, k + 1)
                for t in range(LB * k, LB * (k + 1)):
                    last = nc.scalar.activation(h_sb[:, t, :], x_sb[:, t, :], ACT.Relu, bias=shift[:, t:t + 1],
                                                scale=rstd[:, t:t + 1])
                last.then_inc(h_ready, 1)

            def copy_hT(k):
                act.wait_ge(hT_in_psum, k + 1)
                nc.scalar.copy(hT[:, :, 512 * k:512 * (k + 1)],
                               pair[k % 2].rearrange("p (f j) -> p f j", f=KC)).then_inc(hT_ready, 1)

            root(0)
            root(1)
            for k in range(BATCHES):
                normalise(k)
                if k + 2 < BATCHES:
                    root(k + 2)
                if k >= 1:
                    copy_hT(k - 1)
            copy_hT(BATCHES - 1)

            def relu(n, h):
                if isinstance(n, int) and n < HEADS:
                    act.wait_ge(dst_ready, 2 * h + 2)
                    if n == 0:
                        act.wait_ge(src_ready, 1)
                    if n == 2:
                        act.wait_ge(rows_ready, BATCHES)
                wait(act, transposed, 2 * (n - HEADS) + 2)
                nc.scalar.activation(e[:, h, :], dst_rows[:, h, :], ACT.Relu, bias=src_col[:, bass.ds(n, 1)],
                                     scale=(1 - SLOPE) / SLOPE).then_inc(relu_done, 1)

            def exp(n, h, u, t):
                act.wait_ge(max_done, n + 1)
                if h == 0:
                    wait(act, inv_done, t)
                nc.scalar.activation(e[:, h, :], e[:, h, :], ACT.Exp, bias=neg_max[:, h:h + 1], scale=-1.0,
                                     accum_out=row_sum[:, u, h:h + 1]).then_inc(exp_done, 1)

            def split_hi(t, u, g):
                h, half = g // 2, g % 2
                act.wait_ge(transposed, GROUPS * t + g + 1)
                if g == 0:
                    wait(act, u_done, KC * (t - 1))
                nc.scalar.activation(wt[:, u, 0, HALF * half:HALF * (half + 1), h * P:(h + 1) * P],
                                     tp[:, g % 2, :].rearrange("p (c i) -> p c i", c=HALF),
                                     ACT.Copy, scale=W_SCALE).then_inc(hi_by_act, 1)

            def copy_u(t, f):
                act.wait_ge(u_done, KC * t + f + 1)
                wait(act, final_done, t)
                nc.scalar.copy(u_sb[:, f, :], u_ps[:, f, :]).then_inc(u_copied, 1)

            def slot(t, u, h):
                if 2 * h not in HI_ON_DVE:
                    split_hi(t, u, 2 * h)
                static = isinstance(t, int)
                if h == 0 and not (static and t < 2):
                    copy_u(t - 2, 1)
                if h == 2 and not (static and t < 1):
                    copy_u(t - 1, 0)
                h1, h3 = (h + 1) % HEADS, (h + 3) % HEADS
                n = HEADS * t + h
                if not (static and n + 1 >= NH):
                    exp(n + 1, h1, u if h1 else 1 - u, t)
                if 2 * h + 1 not in HI_ON_DVE:
                    split_hi(t, u, 2 * h + 1)
                if not (static and n + 3 >= NH):
                    relu(n + 3, h3)

            relu(0, 0)
            relu(1, 1)
            exp(0, 0, 0, 0)
            relu(2, 2)
            for t in range(2):
                for h in range(HEADS):
                    slot(t, t, h)
            with act.Fori(1, TILES // 2 - 1) as p:
                for u in range(2):
                    for h in range(HEADS):
                        slot(2 * p + u, u, h)
            for t in range(TILES - 2, TILES):
                for h in range(HEADS):
                    slot(t, t % 2, h)
            copy_u(TILES - 2, 1)
            copy_u(TILES - 1, 0)
            copy_u(TILES - 1, 1)

        @block.vector
        def _(dve):
            steps = [0]

            def link(ins):
                steps[0] += 1
                ins.then_inc(ln_step, 1)
                dve.wait_ge(ln_step, steps[0])

            def statistics(k):
                dve.wait_ge(x_batch_in[k], 16)
                for t in range(LB * k, LB * (k + 1)):
                    last = nc.vector.bn_stats(stats[:, t, :], x_sb[:, t, :])
                link(last)
                for t in range(LB * k, LB * (k + 1)):
                    last = nc.vector.bn_aggr(mean_var[:, t, :], stats[:, t, :])
                link(last)
                nc.vector.tensor_scalar(var_eps[:, LB * k:LB * (k + 1)], mean_var[:, LB * k:LB * (k + 1), 1], EPS,
                                        None, ALU.add).then_inc(var_ready, 1)

            def scale_and_shift(k):
                batch = slice(LB * k, LB * (k + 1))
                dve.wait_ge(std_ready, k + 1)
                link(nc.vector.reciprocal(rstd[:, batch], std[:, batch]))
                link(nc.vector.tensor_tensor(newton[:, batch], rstd[:, batch], rstd[:, batch], ALU.mult))
                link(nc.vector.tensor_tensor(newton[:, batch], newton[:, batch], var_eps[:, batch], ALU.mult))
                link(nc.vector.tensor_scalar(newton[:, batch], newton[:, batch], -0.5 * H_SCALE, 1.5 * H_SCALE,
                                             ALU.mult, ALU.add))
                link(nc.vector.tensor_tensor(rstd[:, batch], rstd[:, batch], newton[:, batch], ALU.mult))
                nc.vector.scalar_tensor_tensor(shift[:, batch], mean_var[:, batch, 0], -1.0, rstd[:, batch],
                                               ALU.mult, ALU.mult).then_inc(norm_ready, 1)

            statistics(0)
            for k in range(BATCHES):
                if k + 1 < BATCHES:
                    statistics(k + 1)
                scale_and_shift(k)
            dve.wait_ge(w_in, 16)
            dve.wait_ge(a_in, 16)
            for k in range(KC):
                for s in range(2):
                    for h in range(HEADS):
                        c = s * HEADS + h
                        last = nc.vector.tensor_tensor_reduce(
                            prod[:, k * 2 * HEADS + c, :], w_sb[:, k, h * D:(h + 1) * D], a_sb[:, h, s, :], 1.0, 0.0,
                            ALU.mult, ALU.add, wa[:, k, c:c + 1])
            last.then_inc(wa_ready, 1)
            for k in range(BATCHES):
                dve.wait_ge(rows_in_psum, k + 1)
                nc.vector.tensor_copy(rows[:, 512 * k:512 * (k + 1)],
                                      rows_ps[:, 512 * k:512 * (k + 1)]).then_inc(rows_ready, 1)

            def copy_dst(r):
                h, half = r // 2, r % 2
                dve.wait_ge(dst_in_psum, r + 1)
                nc.vector.tensor_scalar(dst_rows[:, h, half * (N // 2):(half + 1) * (N // 2)], pair[r % 2], SLOPE / H_SCALE,
                                        None, ALU.mult).then_inc(dst_ready, 1)

            def wait_scores(n):
                dve.wait_ge(relu_done, n + 1)
                dve.wait_ge(biased_done, n + 1)
                wait(dve, exp_done, n - HEADS + 1)

            def scores(h):
                nc.vector.tensor_tensor_reduce(e[:, h, :], e[:, h, :], biased[:, h % 2, :], -1.0, FLT_MAX, ALU.add,
                                               ALU.min, neg_max[:, h:h + 1]).then_inc(max_done, 1)

            copy_dst(0)
            copy_dst(1)
            dve.wait_ge(src_in_psum, 1)
            nc.vector.tensor_scalar(src_col[:, :].rearrange("p (t h) -> p t h", t=TILES), src_ps[:, :, 0:HEADS],
                                    (1 - SLOPE) / H_SCALE, None, ALU.mult).then_inc(src_ready, 1)
            for q in range(2, 2 * HEADS):
                copy_dst(q)
                if q == 3 or q == 5:
                    wait_scores((q - 3) // 2)
                    scores((q - 3) // 2)

            def act_his(g):
                return sum(1 for k in range(g + 1) if k not in HI_ON_DVE)

            def split(t, u, g):
                h, half = g // 2, g % 2
                hi = wt[:, u, 0, HALF * half:HALF * (half + 1), h * P:(h + 1) * P]
                lo = wt[:, u, 1, HALF * half:HALF * (half + 1), h * P:(h + 1) * P]
                group = tp[:, g % 2, :].rearrange("p (c i) -> p c i", c=HALF)
                if g == 0:
                    wait(dve, u_done, KC * (t - 1))
                if g in HI_ON_DVE:
                    dve.wait_ge(transposed, GROUPS * t + g + 1)
                    nc.vector.tensor_scalar(hi, group, W_SCALE, None, ALU.mult).then_inc(hi_by_dve, 1)
                    dve.wait_ge(hi_by_dve, len(HI_ON_DVE) * t + HI_ON_DVE.index(g) + 1)
                else:
                    dve.wait_ge(hi_by_act, act_his(GROUPS - 1) * t + act_his(g))
                nc.vector.scalar_tensor_tensor(lo, group, W_SCALE, hi, ALU.mult, ALU.subtract).then_inc(lo_done, 1)

            def invert_sums(t, u):
                dve.wait_ge(exp_done, HEADS * (t + 1))
                wait(dve, acc_done, t - 1)
                nc.vector.tensor_scalar(row_inv[:, u, :], row_sum[:, u, :], HEADS * H_SCALE * W_SCALE, None,
                                        ALU.mult).then_inc(inv_step, 1)
                dve.wait_ge(inv_step, t + 1)
                nc.vector.reciprocal(row_inv[:, u, :], row_inv[:, u, :]).then_inc(inv_done, 1)

            def output(t, u, p):
                dve.wait_ge(final_done, t + 1)
                dve.wait_ge(inv_done, t + 1)
                dve.wait_ge(x_res_in[u], 16 * (p + 1))
                wait(dve, out_written[u], 16 * p)
                for h in range(HEADS):
                    last = nc.vector.scalar_tensor_tensor(
                        o_sb[:, u, :], f_ps[:, h, :], row_inv[:, u, h:h + 1], x_res[:, u, :] if h == 0 else o_sb[:, u, :],
                        ALU.mult, ALU.add)
                    if h < HEADS - 1:
                        last.then_inc(acc_step, 1)
                        dve.wait_ge(acc_step, (HEADS - 1) * t + h + 1)
                last.then_inc(acc_done, 1)

            def slot(t, u, p, h):
                static = isinstance(t, int)
                n = HEADS * t + h
                more = not (static and n + 2 >= NH)
                h2 = (h + 2) % HEADS
                if more:
                    wait_scores(n + 2)
                split(t, u, 2 * h)
                if more:
                    scores(h2)
                split(t, u, 2 * h + 1)
                if h == 0 and not (static and t < 1):
                    invert_sums(t - 1, 1 - u)
                if h == 1 and not (static and t < 2):
                    output(t - 2, u, p - 1)

            for t in range(2):
                for h in range(HEADS):
                    slot(t, t, 0, h)
            with dve.Fori(1, TILES // 2 - 1) as p:
                for u in range(2):
                    for h in range(HEADS):
                        slot(2 * p + u, u, p, h)
            for t in range(TILES - 2, TILES):
                for h in range(HEADS):
                    slot(t, t % 2, t // 2, h)
            invert_sums(TILES - 1, 1)
            output(TILES - 2, 0, TILES // 2 - 1)
            output(TILES - 1, 1, TILES // 2 - 1)


_INS = ['x', 'adj', 'L0_gnn_W', 'L0_gnn_a']


def kernel(**inputs):
    import numpy as _np
    import concourse.bacc as _bacc
    from concourse import mybir as _mybir
    from concourse.bass_utils import run_bass_kernel_spmd as _run

    nc = _bacc.Bacc("TRN2", target_bir_lowering=False, num_devices=1)
    arrays, args = {}, []
    for name in _INS:
        arr = _np.ascontiguousarray(inputs[name])
        arrays[f"in_{name}_dram"] = arr
        args.append(nc.dram_tensor(f"in_{name}_dram", arr.shape, _mybir.dt.from_np(arr.dtype), kind="ExternalInput").ap())
    out = nc.dram_tensor("out_dram", inputs['x'].shape, _mybir.dt.float32, kind="ExternalOutput").ap()
    gat_layer(nc, *args, out)
    r = _run(nc, [arrays], core_ids=[0])
    return r.results[0]["out_dram"]
```

```python
from contextlib import ExitStack

import concourse.bass as bass
from concourse import mybir

ALU = mybir.AluOpType
ACT = mybir.ActivationFunctionType
F32 = mybir.dt.float32
F16 = mybir.dt.float16
BF16 = mybir.dt.bfloat16
I32 = mybir.dt.int32
AX = mybir.AxisListType

P = 128
EPS = 1e-5
FLT_MAX = 3.4028235e38
SLOPE = 0.01
H_SCALE = 2.0 ** 11
W_SCALE = 2.0 ** 14
U_SCALE = 1.0 / (H_SCALE * W_SCALE)
W_RANGE = 2.0 ** 14
W_LEAST = 1e-32
EXPONENT_BITS = 0x7F800000


def gat_layer(nc, x, adj, W, a, out):
    N, F = x.shape
    HEADS, D2, _ = a.shape
    D = D2 // 2
    TILES = N // P
    KC = F // P
    HALF = TILES // 2
    B = 32
    Q = P // B
    BC = 512 // P
    PARTS = 8
    SHUFFLED = 2
    GROUPS = 2 * (HEADS - SHUFFLED)
    NH = HEADS * TILES
    LB = 4
    BATCHES = TILES // LB
    DBLK = N // 2 // 512
    MM_PER_PART = KC * TILES // PARTS
    assert HEADS == 4 and KC == 2 and D == F and N == 2048
    SHUFFLE_INC = 16 * Q * Q
    PART_AT = [0, 64, 96]
    ROWS = PART_AT[-1] + 2 * HEADS

    ctx = ExitStack()
    with ctx:
        def sb(name, shape, dt):
            return ctx.enter_context(nc.sbuf_tensor(name, shape, dt))

        def sem(name):
            return ctx.enter_context(nc.semaphore(name))

        dst_rows = sb("dst_rows", [P, HEADS, N], F32)
        h_hi = sb("h_hi", [P, TILES, F], F16)
        h_lo = sb("h_lo", [P, TILES, F], F16)
        w16 = sb("w16", [P, 2, KC, HEADS * D], F16)
        src_col = sb("src_col", [P, NH], F32)
        adj_sb = sb("adj_sb", [P, 2, N], F32)
        e = sb("e", [P, HEADS, N], F32)
        wt = sb("wt", [P, 2, 2, HEADS, TILES // BC, Q, BC, B], F16)
        blocks = sb("blocks", [P, SHUFFLED, Q, TILES * B], F32)
        whole = sb("whole", [P, SHUFFLED, Q, TILES * B], F32)
        u16 = sb("u16", [P, 2, KC, HEADS * P], F16)
        neg_max = sb("neg_max", [P, HEADS], F32)
        row_sum = sb("row_sum", [P, 2, HEADS], F32)
        row_inv = sb("row_inv", [P, 2, HEADS], F32)
        x_out = sb("x_out", [P, 2, F], F32)
        w_scale = sb("w_scale", [P, 1], F32)
        warm = sb("warm", [P, 1], F32)
        ident = sb("ident", [P, P], F32)
        mean_var = sb("mean_var", [P, TILES, 2], F32)
        stats = sb("stats", [P, TILES, 6], F32)
        var_eps = sb("var_eps", [P, TILES], F32)
        std = sb("std", [P, TILES], F32)
        rstd = sb("rstd", [P, TILES], F32)
        newton = sb("newton", [P, TILES], F32)
        shift = sb("shift", [P, TILES], F32)
        def setup_half(buffer, part):
            return wt[:, buffer, part].rearrange("p h c a d i -> p (h c a d i)").bitcast(F32)

        spare = whole[:, 0].rearrange("p a x -> p (a x)")
        pick = spare[0:ROWS, 512:512 + HEADS * P // 2].bitcast(BF16).rearrange("p (h m) -> p h m", h=HEADS)
        pick_col = spare[0:ROWS, 1024:1024 + HEADS]
        w_max, w_top = spare[:, 1280:1281], spare[:, 1281:1282]
        w_sb = blocks[:, 1].rearrange("p b x -> p (b x)").rearrange("p (k n) -> p k n", k=KC)
        wa = spare[:, 0:KC * ROWS].rearrange("p (k r) -> p k r", k=KC)
        rest = whole[0:ROWS, 1].rearrange("p a x -> p (a x)")
        x_sb = setup_half(0, 0).rearrange("p (t f) -> p t f", t=TILES)
        h_sb = setup_half(0, 1).rearrange("p (t f) -> p t f", t=TILES)
        a_sb = setup_half(1, 0)[:, 0:HEADS * 2 * D].rearrange("p (h s d) -> p h s d", h=HEADS, s=2)
        prod = setup_half(1, 1).rearrange("p (k d) -> p k d", d=D)
        rows = setup_half(1, 0)[0:2 * HEADS, N:2 * N]
        row_parts = setup_half(1, 1)[0:ROWS, 0:N // 2].bitcast(BF16)
        hT = e[:, 2:4, :]

        tp = ctx.enter_context(nc.psum_tensor("tp", [P, 2, HALF * P], F32))
        u_ps = ctx.enter_context(nc.psum_tensor("u_ps", [P, KC, HEADS * P], F32))
        f_ps = ctx.enter_context(nc.psum_tensor("f_ps", [P, HEADS, D], F32))
        pair = [u_ps[:, :, :].rearrange("p k m -> p (k m)"), f_ps[:, :, :].rearrange("p h d -> p (h d)")]
        src_ps = tp[:, 0, 0:TILES * 2 * HEADS].rearrange("p (t c) -> p t c", t=TILES)
        rows_ps = tp[:, :, :].rearrange("p a m -> p (a m)")[0:ROWS, :]

        x_batch_in = [sem(f"x_batch_in{k}") for k in range(BATCHES)]
        w_in = sem("w_in")
        a_in = sem("a_in")
        adj_in = [sem(f"adj_in{u}") for u in range(2)]
        x_in = [sem(f"x_in{u}") for u in range(2)]
        out_written = [sem(f"out_written{u}") for u in range(2)]
        ident_zero = sem("ident_zero")
        ident_ready = sem("ident_ready")
        ln_step = sem("ln_step")
        var_ready = sem("var_ready")
        std_ready = sem("std_ready")
        norm_ready = sem("norm_ready")
        h_ready = sem("h_ready")
        hT_in_psum = sem("hT_in_psum")
        hT_ready = sem("hT_ready")
        h_split = sem("h_split")
        h_hi_ready = sem("h_hi_ready")
        wa_ready = sem("wa_ready")
        pick_step = sem("pick_step")
        pick_ready = sem("pick_ready")
        rows_in_psum = sem("rows_in_psum")
        rows_ready = sem("rows_ready")
        src_in_psum = sem("src_in_psum")
        src_ready = sem("src_ready")
        dst_in_psum = sem("dst_in_psum")
        dst_ready = [sem(f"dst_ready{half}") for half in range(2)]
        first_parts = sem("first_parts")
        parts_step = sem("parts_step")
        parts_ready = sem("parts_ready")
        wa_zero = sem("wa_zero")
        wa_step = sem("wa_step")
        relu_done = sem("relu_done")
        leaky_by_dve = sem("leaky_by_dve")
        leaky_done = sem("leaky_done")
        max_done = sem("max_done")
        exp_done = sem("exp_done")
        transposed = sem("transposed")
        blocks_done, shuffled, hi_of_shuffle, lo_of_shuffle = [
            [sem(f"{what}{h}") for h in range(SHUFFLED)]
            for what in ("blocks_done", "shuffled", "hi_of_shuffle", "lo_of_shuffle")]
        hi_of_group = sem("hi_of_group")
        lo_of_group = sem("lo_of_group")
        u_done = sem("u_done")
        u_hi_done = sem("u_hi_done")
        u_split = sem("u_split")
        w_max_ready = sem("w_max_ready")
        w_max_spread = sem("w_max_spread")
        scale_step = sem("scale_step")
        w_hi_ready = sem("w_hi_ready")
        w_split = sem("w_split")
        final_done = sem("final_done")
        inv_step = sem("inv_step")
        inv_done = sem("inv_done")
        acc_step = sem("acc_step")
        acc_done = sem("acc_done")

        block = ctx.enter_context(nc.Block())

        def half_head(u, part, h, half):
            n = HALF // BC
            return wt[:, u, part, h, n * half:n * (half + 1)].rearrange("p c a d i -> p (c a d i)")

        def head_of(t, g):
            return g // 2 if isinstance(t, int) and t == 0 else g // 2 + SHUFFLED

        def groups_before(t, g):
            return g if isinstance(t, int) and t == 0 else GROUPS * t + g + 2 * SHUFFLED

        def groups_of(t, h, half):
            first = isinstance(t, int) and t == 0
            return groups_before(t, 2 * (h if first else h - SHUFFLED) + half) + 1

        def wait(eng, s, count):
            if not (isinstance(count, int) and count <= 0):
                eng.wait_ge(s, count)

        x_t = x.rearrange("(t p) f -> p t f", p=P)

        @block.sync
        def _(sp):
            for k in range(BATCHES):
                sp.dma_start(x_sb[:, LB * k:LB * (k + 1), :], x_t[:, LB * k:LB * (k + 1), :]).then_inc(
                    x_batch_in[k], 16)
            sp.dma_start(w_sb[:, :, :], W.rearrange("(k p) n -> p k n", p=P)).then_inc(w_in, 16)
            sp.dma_start(a_sb.rearrange("p h s d -> p (h s d)"), a.rearrange("h d o -> o (h d)").to_broadcast(
                [P, HEADS * 2 * D])).then_inc(a_in, 16)

            def load_x(t, u, p):
                wait(sp, out_written[u], 16 * p)
                sp.dma_start(x_out[:, u, :], x[bass.ts(t, P), :]).then_inc(x_in[u], 16)

            def store(t, u):
                sp.wait_ge(acc_done, t + 1)
                sp.dma_start(out[bass.ts(t, P), :], x_out[:, u, :]).then_inc(out_written[u], 16)

            def shuffle(t, h):
                wait(sp, lo_of_shuffle[h], t - 1)
                sp.wait_ge(blocks_done[h], t)
                for q in range(Q):
                    for b in range(Q):
                        sp.dma_start(whole[B * b:B * (b + 1), h, q, :],
                                     blocks[B * q:B * (q + 1), h, b, :]).then_inc(shuffled[h], 16)

            def load_adj(t, u):
                wait(sp, max_done, HEADS * (t - 1))
                sp.dma_start(adj_sb[:, u, :], adj[bass.ts(t, P), :]).then_inc(adj_in[u], 16)

            def step(t, u, p, more=True):
                shuffle(t, 0)
                if not (isinstance(t, int) and t < 3):
                    load_x(t - 1, 1 - u, p - 1 + u)
                shuffle(t, 1)
                store(t - 2, u)
                if more:
                    load_adj(t + 2, u)

            load_adj(0, 0)
            load_adj(1, 1)
            load_x(0, 0, 0)
            load_x(1, 1, 0)
            load_adj(2, 0)
            shuffle(1, 0)
            load_adj(3, 1)
            shuffle(1, 1)
            for t in (2, 3):
                step(t, t - 2, 1)
            with sp.Fori(2, TILES // 2 - 1) as p:
                for u in range(2):
                    step(2 * p + u, u, p)
            for u in range(2):
                step(TILES - 2 + u, u, TILES // 2 - 1, more=False)
            load_x(TILES - 1, 1, TILES // 2 - 1)
            store(TILES - 2, 0)
            store(TILES - 1, 1)
            for u in range(2):
                sp.wait_ge(out_written[u], 16 * (TILES // 2))

        @block.gpsimd
        def _(pool):
            nc.gpsimd.memset(ident[:, :], 0.0).then_inc(ident_zero, 1)
            pool.wait_ge(ident_zero, 1)
            nc.gpsimd.affine_select(out=ident[:, :], in_=ident[:, :], compare_op=ALU.not_equal, fill=1.0,
                                    base=0, pattern=[[-1, P]], channel_multiplier=1).then_inc(ident_ready, 1)
            nc.gpsimd.memset(wa[:, :, :], 0.0).then_inc(wa_zero, 1)
            pool.wait_ge(ident_ready, 1)
            at = [p + HEADS for p in PART_AT]
            nc.gpsimd.tensor_tensor(pick_col, ident[0:ROWS, at[0]:at[0] + HEADS], ident[0:ROWS, at[1]:at[1] + HEADS],
                                    ALU.add).then_inc(pick_step, 1)
            pool.wait_ge(pick_step, 1)
            nc.gpsimd.tensor_tensor(pick_col, pick_col, ident[0:ROWS, at[2]:at[2] + HEADS],
                                    ALU.add).then_inc(pick_step, 1)
            pool.wait_ge(pick_step, 2)
            nc.gpsimd.tensor_copy(pick[:, :, :], pick_col.unsqueeze(2).to_broadcast([ROWS, HEADS, P])).then_inc(
                pick_ready, 1)
            for k in range(BATCHES):
                batch = slice(LB * k, LB * (k + 1))
                pool.wait_ge(h_ready, k + 1)
                nc.gpsimd.tensor_copy(h_hi[:, batch, :], h_sb[:, batch, :]).then_inc(h_hi_ready, 1)
                pool.wait_ge(h_hi_ready, k + 1)
                nc.gpsimd.tensor_tensor(h_lo[:, batch, :], h_sb[:, batch, :], h_hi[:, batch, :],
                                        ALU.subtract).then_inc(h_split, 1)

            def add_slope(t, h):
                pool.wait_ge(relu_done, HEADS * t + h + 1)
                nc.gpsimd.tensor_tensor(e[:, h, :], e[:, h, :], dst_rows[:, h, :], ALU.add).then_inc(leaky_done, 1)

            for h in range(1, HEADS, 2):
                add_slope(0, h)
            with pool.Fori(1, TILES) as t:
                for h in range(HEADS):
                    add_slope(t, h)

        @block.tensor
        def _(pe):
            def transpose_group(t, g):
                h, half = head_of(t, g), g % 2
                pe.wait_ge(exp_done, HEADS * t + h + 1)
                wait(pe, lo_of_group, groups_before(t, g) - 1)
                group = tp[:, g % 2, :].rearrange("p (c a d i) -> p c d a i", a=Q, d=BC, i=B)
                for b in range(HALF):
                    c = HALF * half + b
                    last = pe.transpose(group[:, b // BC, b % BC], e[:, h, c * P:(c + 1) * P], ident[:, :])
                last.then_inc(transposed, 1)

            def weighted_sum(t, u, part):
                f, quarter = part // (PARTS // KC), part % (PARTS // KC)
                if part == 0:
                    for h in range(SHUFFLED):
                        wait(pe, lo_of_shuffle[h], t)
                    pe.wait_ge(lo_of_group, groups_of(t, HEADS - 1, 0))
                if part == 2:
                    pe.wait_ge(lo_of_group, groups_of(t, HEADS - 1, 1))
                if quarter == 0:
                    wait(pe, u_split, KC * (t - 1) + f + 1)
                for c in range(MM_PER_PART * quarter, MM_PER_PART * (quarter + 1)):
                    h_parts = [x[:, c, f * P:(f + 1) * P] for x in (h_hi, h_lo)]
                    w_parts = [wt[:, u, x, :, c // BC, :, c % BC, :] for x in range(2)]
                    pe.matmul(u_ps[:, f, :], h_parts[0], w_parts[0], start=(c == 0), stop=False)
                    pe.matmul(u_ps[:, f, :], h_parts[0], w_parts[1], start=False, stop=False)
                    last = pe.matmul(u_ps[:, f, :], h_parts[1], w_parts[0], start=False, stop=(c == TILES - 1))
                if quarter == PARTS // KC - 1:
                    last.then_inc(u_done, 1)

            def final_products(t):
                if isinstance(t, int) and t == 0:
                    pe.wait_ge(w_split, 1)
                pe.wait_ge(u_split, KC * (t + 1))
                wait(pe, acc_done, t)
                for h in range(HEADS):
                    passes = [(k, x, y) for k in range(KC) for x, y in ((0, 0), (0, 1), (1, 0))]
                    for n, (k, x, y) in enumerate(passes):
                        last = pe.matmul(f_ps[:, h, :], u16[:, x, k, h * P:(h + 1) * P],
                                         w16[:, y, k, h * D:(h + 1) * D],
                                         start=(n == 0), stop=(n == len(passes) - 1))
                last.then_inc(final_done, 1)

            def step(t, u, transposes=True, sums=True):
                for part in range(PARTS // 2, PARTS):
                    weighted_sum(t - 2, u, part)
                if transposes:
                    transpose_group(t, 0)
                    transpose_group(t, 1)
                if sums:
                    weighted_sum(t - 1, 1 - u, 0)
                final_products(t - 2)
                if sums:
                    weighted_sum(t - 1, 1 - u, 1)
                if transposes:
                    transpose_group(t, 2)
                if sums:
                    weighted_sum(t - 1, 1 - u, 2)
                if transposes:
                    transpose_group(t, 3)
                if sums:
                    weighted_sum(t - 1, 1 - u, 3)

            pe.wait_ge(ident_ready, 1)
            for k in range(BATCHES):
                pe.wait_ge(h_ready, k + 1)
                wait(pe, hT_ready, k - 1)
                for f in range(KC):
                    for b in range(LB):
                        at = (f * LB + b) * P
                        last = pe.transpose(pair[k % 2][:, at:at + P], h_sb[:, LB * k + b, f * P:(f + 1) * P],
                                            ident[:, :])
                last.then_inc(hT_in_psum, 1)
            pe.wait_ge(wa_ready, 1)
            for k in range(BATCHES):
                pe.wait_ge(hT_ready, k + 1)
                for f in range(KC):
                    last = pe.matmul(rows_ps[:, 512 * k:512 * (k + 1)], wa[:, f, :],
                                     hT[:, f, 512 * k:512 * (k + 1)], start=(f == 0), stop=(f == KC - 1))
                last.then_inc(rows_in_psum, 1)
                if k == 1:
                    pe.wait_ge(w_max_ready, 1)
                    pe.wait_ge(hT_ready, BATCHES)
                    pe.matmul(pair[1][:, 0:P], w_max.to_broadcast([P, P]), ident[:, :], start=True,
                              stop=True).then_inc(w_max_spread, 1)

            def spread_dst(q):
                h, half = q // 2, q % 2
                pe.wait_ge(parts_ready, BATCHES // 2 * (half + 1))
                wait(pe, dst_ready[half], h)
                if q == 1:
                    pe.wait_ge(scale_step, 1)
                for b in range(DBLK):
                    j = (half * DBLK + b) * 512
                    last = pe.matmul(pair[q % 2][:, b * 512:(b + 1) * 512], pick[:, h, :], row_parts[:, j:j + 512],
                                     start=True, stop=True)
                last.then_inc(dst_in_psum, 1)

            pe.wait_ge(pick_ready, 1)
            spread_dst(0)
            for t in range(TILES):
                if t % LB == 0:
                    pe.wait_ge(rows_ready, t // LB + 1)
                last = pe.transpose(src_ps[:, t, :], rows[:, t * P:(t + 1) * P], ident[0:2 * HEADS, 0:2 * HEADS])
            last.then_inc(src_in_psum, 1)
            for q in range(1, 2 * HEADS):
                spread_dst(q)
            pe.wait_ge(h_split, BATCHES)
            for half in range(2):
                pe.wait_ge(dst_ready[half], HEADS)
            for g in range(2 * HEADS):
                transpose_group(0, g)
            weighted_sum(0, 0, 0)
            weighted_sum(0, 0, 1)
            transpose_group(1, 0)
            transpose_group(1, 1)
            weighted_sum(0, 0, 2)
            transpose_group(1, 2)
            transpose_group(1, 3)
            weighted_sum(0, 0, 3)
            for t in (2, 3):
                step(t, t - 2)
            with pe.Fori(2, TILES // 2) as p:
                for u in range(2):
                    step(2 * p + u, u)
            step(TILES, 0, transposes=False)
            step(TILES + 1, 1, transposes=False, sums=False)

        @block.scalar
        def _(act):
            def root(k):
                act.wait_ge(var_ready, k + 1)
                nc.scalar.activation(std[:, LB * k:LB * (k + 1)], var_eps[:, LB * k:LB * (k + 1)],
                                     ACT.Sqrt).then_inc(std_ready, 1)

            def normalise(k):
                act.wait_ge(norm_ready, k + 1)
                for t in range(LB * k, LB * (k + 1)):
                    last = nc.scalar.activation(h_sb[:, t, :], x_sb[:, t, :], ACT.Relu, bias=shift[:, t:t + 1],
                                                scale=rstd[:, t:t + 1])
                last.then_inc(h_ready, 1)

            def copy_hT(k):
                act.wait_ge(hT_in_psum, k + 1)
                nc.scalar.copy(hT[:, :, 512 * k:512 * (k + 1)],
                               pair[k % 2].rearrange("p (f j) -> p f j", f=KC)).then_inc(hT_ready, 1)

            root(0)
            root(1)
            for k in range(BATCHES):
                normalise(k)
                if k + 2 < BATCHES:
                    root(k + 2)
                if k >= 1:
                    copy_hT(k - 1)
            act.wait_ge(std_ready, BATCHES)
            nc.scalar.activation(warm[:, :], std[:, 0:1], ACT.Exp)
            copy_hT(BATCHES - 1)

            def copy_rows(k):
                act.wait_ge(parts_step, 2 * k + 1)
                nc.scalar.copy(rows[:, 512 * k:512 * (k + 1)],
                               rows_ps[0:2 * HEADS, 512 * k:512 * (k + 1)]).then_inc(rows_ready, 1)

            for k in range(BATCHES):
                act.wait_ge(rows_in_psum, k + 1)
                nc.scalar.copy(row_parts[:, 512 * k:512 * (k + 1)],
                               rows_ps[:, 512 * k:512 * (k + 1)]).then_inc(first_parts, 1)
                if k >= 1:
                    copy_rows(k - 1)
            copy_rows(BATCHES - 1)

            def copy_dst(h):
                act.wait_ge(dst_in_psum, 2 * h + 1)
                nc.scalar.mul(dst_rows[:, h, 0:N // 2], pair[0], SLOPE / H_SCALE).then_inc(dst_ready[0], 1)

            def relu(t, h):
                if isinstance(t, int) and t == 0:
                    for half in range(2):
                        act.wait_ge(dst_ready[half], h + 1)
                    if h == 0:
                        act.wait_ge(src_ready, 1)
                    if h == 2:
                        act.wait_ge(rows_ready, BATCHES)
                if h < SHUFFLED and not (isinstance(t, int) and t == 1):
                    wait(act, blocks_done[h], t - 1)
                elif not (isinstance(t, int) and t == 0):
                    act.wait_ge(transposed, groups_of(t - 1, h, 1))
                nc.scalar.activation(e[:, h, :], dst_rows[:, h, :], ACT.Relu,
                                     bias=src_col[:, bass.ds(HEADS * t + h, 1)],
                                     scale=(1 - SLOPE) / SLOPE).then_inc(relu_done, 1)

            def exp(t, u, h):
                act.wait_ge(max_done, HEADS * t + h + 1)
                if h == 0:
                    wait(act, inv_done, t - 1)
                nc.scalar.activation(e[:, h, :], e[:, h, :], ACT.Exp, bias=neg_max[:, h:h + 1], scale=-1.0,
                                     accum_out=row_sum[:, u, h:h + 1]).then_inc(exp_done, 1)

            def hi_group(t, u, g):
                h, half = head_of(t, g), g % 2
                act.wait_ge(transposed, groups_before(t, g) + 1)
                wait(act, u_done, KC * (t - 1))
                nc.scalar.activation(half_head(u, 0, h, half), tp[:, g % 2, :], ACT.Copy, scale=W_SCALE).then_inc(
                    hi_of_group, 1)

            def hi_shuffle(t, u, h):
                act.wait_ge(shuffled[h], SHUFFLE_INC * t)
                wait(act, u_done, KC * (t - 1))
                nc.scalar.activation(wt[:, u, 0, h].rearrange("p c a d i -> p a c (d i)"),
                                     whole[:, h].rearrange("p a (c x) -> p a c x", x=BC * B), ACT.Copy,
                                     scale=W_SCALE).then_inc(hi_of_shuffle[h], 1)

            def hi_u(t, f):
                act.wait_ge(u_done, KC * t + f + 1)
                wait(act, final_done, t)
                nc.scalar.activation(u16[:, 0, f, :], u_ps[:, f, :], ACT.Copy, scale=U_SCALE).then_inc(
                    u_hi_done, 1)

            def hi_w():
                act.wait_ge(scale_step, 4)
                nc.scalar.activation(w16[:, 0], w_sb, ACT.Copy, scale=w_scale[:, 0:1]).then_inc(w_hi_ready, 1)

            def step(t, u, more=True):
                hi_u(t - 2, 0)
                relu(t, 3)
                exp(t, u, 1)
                hi_shuffle(t - 1, 1 - u, 1)
                exp(t, u, 2)
                if more:
                    relu(t + 1, 0)
                hi_u(t - 2, 1)
                hi_group(t, u, 0)
                hi_group(t, u, 1)
                exp(t, u, 3)
                if more:
                    relu(t + 1, 1)
                hi_group(t, u, 2)
                hi_shuffle(t, u, 0)
                if more:
                    relu(t + 1, 2)
                hi_group(t, u, 3)
                if more:
                    exp(t + 1, 1 - u, 0)

            copy_dst(0)
            hi_w()
            copy_dst(1)
            relu(0, 0)
            relu(0, 1)
            copy_dst(2)
            relu(0, 2)
            copy_dst(3)
            exp(0, 0, 0)
            relu(0, 3)
            hi_group(0, 0, 0)
            hi_group(0, 0, 1)
            exp(0, 0, 1)
            relu(1, 0)
            hi_group(0, 0, 2)
            relu(1, 1)
            exp(0, 0, 2)
            hi_group(0, 0, 3)
            exp(0, 0, 3)
            hi_group(0, 0, 4)
            hi_group(0, 0, 5)
            relu(1, 2)
            exp(1, 1, 0)
            hi_group(0, 0, 6)
            relu(1, 3)
            hi_group(0, 0, 7)
            exp(1, 1, 1)
            relu(2, 0)
            exp(1, 1, 2)
            relu(2, 1)
            exp(1, 1, 3)
            hi_group(1, 1, 0)
            hi_group(1, 1, 1)
            hi_shuffle(1, 1, 0)
            hi_group(1, 1, 2)
            relu(2, 2)
            hi_group(1, 1, 3)
            exp(2, 0, 0)
            for t in (2, 3):
                step(t, t - 2)
            with act.Fori(2, TILES // 2 - 1) as p:
                for u in range(2):
                    step(2 * p + u, u)
            step(TILES - 2, 0)
            step(TILES - 1, 1, more=False)
            hi_u(TILES - 2, 0)
            hi_shuffle(TILES - 1, 1, 1)
            hi_u(TILES - 2, 1)
            hi_u(TILES - 1, 0)
            hi_u(TILES - 1, 1)

        @block.vector
        def _(dve):
            steps = [0]

            def link(ins):
                steps[0] += 1
                ins.then_inc(ln_step, 1)
                dve.wait_ge(ln_step, steps[0])

            def statistics(k):
                dve.wait_ge(x_batch_in[k], 16)
                for t in range(LB * k, LB * (k + 1)):
                    last = nc.vector.bn_stats(stats[:, t, :], x_sb[:, t, :])
                link(last)
                for t in range(LB * k, LB * (k + 1)):
                    last = nc.vector.bn_aggr(mean_var[:, t, :], stats[:, t, :])
                link(last)
                nc.vector.tensor_scalar(var_eps[:, LB * k:LB * (k + 1)], mean_var[:, LB * k:LB * (k + 1), 1], EPS,
                                        None, ALU.add).then_inc(var_ready, 1)

            def scale_and_shift(k):
                batch = slice(LB * k, LB * (k + 1))
                dve.wait_ge(std_ready, k + 1)
                link(nc.vector.reciprocal(rstd[:, batch], std[:, batch]))
                link(nc.vector.tensor_tensor(newton[:, batch], rstd[:, batch], rstd[:, batch], ALU.mult))
                link(nc.vector.tensor_tensor(newton[:, batch], newton[:, batch], var_eps[:, batch], ALU.mult))
                link(nc.vector.tensor_scalar(newton[:, batch], newton[:, batch], -0.5 * H_SCALE, 1.5 * H_SCALE,
                                             ALU.mult, ALU.add))
                link(nc.vector.tensor_tensor(rstd[:, batch], rstd[:, batch], newton[:, batch], ALU.mult))
                nc.vector.scalar_tensor_tensor(shift[:, batch], mean_var[:, batch, 0], -1.0, rstd[:, batch],
                                               ALU.mult, ALU.mult).then_inc(norm_ready, 1)

            statistics(0)
            for k in range(BATCHES):
                if k + 1 < BATCHES:
                    statistics(k + 1)
                scale_and_shift(k)
            dve.wait_ge(w_in, 16)
            dve.wait_ge(a_in, 16)
            dve.wait_ge(wa_zero, 1)
            for k in range(KC):
                for s in range(2):
                    for h in range(HEADS):
                        c = s * HEADS + h
                        last = nc.vector.tensor_tensor_reduce(
                            prod[:, k * 2 * HEADS + c, :], w_sb[:, k, h * D:(h + 1) * D], a_sb[:, h, s, :], 1.0, 0.0,
                            ALU.mult, ALU.add, wa[:, k, c:c + 1])
            last.then_inc(wa_step, 1)
            dve.wait_ge(wa_step, 1)
            for at in PART_AT[1:]:
                last = nc.vector.tensor_copy(wa[:, :, at:at + 2 * HEADS], wa[:, :, 0:2 * HEADS])
            last.then_inc(wa_ready, 1)
            nc.vector.tensor_reduce(w_max, w_sb, AX.XY, ALU.max,
                                    apply_absolute_value=True).then_inc(w_max_ready, 1)

            def find_w_scale():
                dve.wait_ge(scale_step, 1)
                nc.vector.tensor_scalar(w_top, w_top, 1.0 / W_RANGE, W_LEAST, ALU.mult, ALU.max).then_inc(
                    scale_step, 1)
                dve.wait_ge(scale_step, 2)
                nc.vector.tensor_scalar(w_top.bitcast(I32), w_top.bitcast(I32), EXPONENT_BITS, None,
                                        ALU.bitwise_and).then_inc(scale_step, 1)
                dve.wait_ge(scale_step, 3)
                nc.vector.reciprocal(w_scale[:, :], w_top).then_inc(scale_step, 1)

            def last_part(k):
                j = slice(512 * k, 512 * (k + 1))
                dve.wait_ge(parts_step, 2 * k + 2)
                nc.vector.tensor_tensor(row_parts[PART_AT[2]:, j], rest[PART_AT[2]:, j], row_parts[PART_AT[2]:, j],
                                        ALU.subtract).then_inc(parts_ready, 1)

            for k in range(BATCHES):
                j = slice(512 * k, 512 * (k + 1))
                dve.wait_ge(first_parts, k + 1)
                nc.vector.tensor_tensor(rest[PART_AT[1]:, j], rows_ps[PART_AT[1]:, j], row_parts[PART_AT[1]:, j],
                                        ALU.subtract).then_inc(parts_step, 1)
                if k >= 1:
                    last_part(k - 1)
                dve.wait_ge(parts_step, 2 * k + 1)
                nc.vector.tensor_copy(row_parts[PART_AT[1]:, j], rest[PART_AT[1]:, j]).then_inc(parts_step, 1)
            dve.wait_ge(w_max_spread, 1)
            nc.vector.tensor_reduce(w_top, pair[1][:, 0:P], AX.X, ALU.max).then_inc(scale_step, 1)
            last_part(BATCHES - 1)

            def copy_dst(h):
                dve.wait_ge(dst_in_psum, 2 * h + 2)
                nc.vector.tensor_scalar(dst_rows[:, h, N // 2:N], pair[1], SLOPE / H_SCALE, None,
                                        ALU.mult).then_inc(dst_ready[1], 1)

            def wait_scores(t, u, p, h):
                n = HEADS * t + h
                if not (isinstance(t, int) and t == 0):
                    dve.wait_ge(leaky_done, n + 1 - HEADS // 2)
                elif h % 2 == 0:
                    dve.wait_ge(leaky_by_dve, h // 2 + 1)
                else:
                    dve.wait_ge(leaky_done, h // 2 + 1)
                if h == 0:
                    dve.wait_ge(adj_in[u], 16 * (p + 1))

            def scores(u, h):
                nc.vector.tensor_tensor_reduce(e[:, h, :], e[:, h, :], adj_sb[:, u, :], -1.0, FLT_MAX, ALU.add,
                                               ALU.min, neg_max[:, h:h + 1]).then_inc(max_done, 1)

            def transpose_blocks(t, h):
                dve.wait_ge(exp_done, HEADS * t + h + 1)
                wait(dve, shuffled[h], SHUFFLE_INC * (t - 1))
                nc.vector.transpose(blocks[:, h].rearrange("p b (c i) -> p c b i", c=TILES),
                                    e[:, h, :].rearrange("p (c b i) -> p c b i", b=Q, i=B)).then_inc(
                                        blocks_done[h], 1)

            def lo_group(t, u, g):
                h, half = head_of(t, g), g % 2
                hi, lo = [half_head(u, x, h, half) for x in range(2)]
                dve.wait_ge(hi_of_group, groups_before(t, g) + 1)
                nc.vector.scalar_tensor_tensor(lo, tp[:, g % 2, :], W_SCALE, hi,
                                               ALU.mult, ALU.subtract).then_inc(lo_of_group, 1)

            def lo_shuffle(t, u, h):
                hi, lo = [wt[:, u, x, h].rearrange("p c a d i -> p a c (d i)") for x in range(2)]
                w = whole[:, h].rearrange("p a (c x) -> p a c x", x=BC * B)
                dve.wait_ge(hi_of_shuffle[h], t)
                for a in range(Q):
                    last = nc.vector.scalar_tensor_tensor(lo[:, a], w[:, a], W_SCALE, hi[:, a], ALU.mult,
                                                          ALU.subtract)
                last.then_inc(lo_of_shuffle[h], 1)

            def lo_u(t, f):
                dve.wait_ge(u_hi_done, KC * t + f + 1)
                nc.vector.scalar_tensor_tensor(u16[:, 1, f, :], u_ps[:, f, :], U_SCALE, u16[:, 0, f, :],
                                               ALU.mult, ALU.subtract).then_inc(u_split, 1)

            def lo_w():
                dve.wait_ge(w_hi_ready, 1)
                nc.vector.scalar_tensor_tensor(w16[:, 1], w_sb, w_scale[:, 0:1], w16[:, 0],
                                               ALU.mult, ALU.subtract).then_inc(w_split, 1)

            def invert_sums(t, u):
                dve.wait_ge(exp_done, HEADS * (t + 1))
                wait(dve, acc_done, t - 1)
                nc.vector.tensor_scalar(row_inv[:, u, :], row_sum[:, u, :], w_scale[:, 0:1], float(HEADS),
                                        ALU.mult, ALU.mult).then_inc(inv_step, 1)
                dve.wait_ge(inv_step, t + 1)
                nc.vector.reciprocal(row_inv[:, u, :], row_inv[:, u, :]).then_inc(inv_done, 1)

            def output(t, u, p):
                dve.wait_ge(final_done, t + 1)
                dve.wait_ge(inv_done, t + 1)
                dve.wait_ge(x_in[u], 16 * (p + 1))
                for h in range(HEADS):
                    last = nc.vector.scalar_tensor_tensor(
                        x_out[:, u, :], f_ps[:, h, :], row_inv[:, u, h:h + 1], x_out[:, u, :],
                        ALU.mult, ALU.add)
                    if h < HEADS - 1:
                        last.then_inc(acc_step, 1)
                        dve.wait_ge(acc_step, (HEADS - 1) * t + h + 1)
                last.then_inc(acc_done, 1)

            def step(t, u, p, more=True):
                wait_scores(t, u, p, 2)
                lo_u(t - 2, 0)
                scores(u, 2)
                transpose_blocks(t, 0)
                wait_scores(t, u, p, 3)
                lo_shuffle(t - 1, 1 - u, 1)
                scores(u, 3)
                lo_u(t - 2, 1)
                transpose_blocks(t, 1)
                lo_group(t, u, 0)
                output(t - 2, u, p - 1)
                if more:
                    wait_scores(t + 1, 1 - u, p + u, 0)
                lo_group(t, u, 1)
                if more:
                    scores(1 - u, 0)
                lo_group(t, u, 2)
                invert_sums(t - 1, 1 - u)
                if more:
                    wait_scores(t + 1, 1 - u, p + u, 1)
                lo_shuffle(t, u, 0)
                if more:
                    scores(1 - u, 1)
                lo_group(t, u, 3)

            def add_slope(h):
                dve.wait_ge(relu_done, h + 1)
                nc.vector.tensor_tensor(e[:, h, :], e[:, h, :], dst_rows[:, h, :], ALU.add).then_inc(
                    leaky_by_dve, 1)

            dve.wait_ge(src_in_psum, 1)
            nc.vector.tensor_scalar(src_col[:, :].rearrange("p (t h) -> p t h", t=TILES), src_ps[:, :, 0:HEADS],
                                    (1 - SLOPE) / H_SCALE, None, ALU.mult).then_inc(src_ready, 1)
            find_w_scale()
            copy_dst(0)
            copy_dst(1)
            add_slope(0)
            copy_dst(2)
            wait_scores(0, 0, 0, 0)
            scores(0, 0)
            copy_dst(3)
            lo_w()
            wait_scores(0, 0, 0, 1)
            scores(0, 1)
            lo_group(0, 0, 0)
            lo_group(0, 0, 1)
            add_slope(2)
            wait_scores(0, 0, 0, 2)
            scores(0, 2)
            lo_group(0, 0, 2)
            wait_scores(0, 0, 0, 3)
            scores(0, 3)
            lo_group(0, 0, 3)
            wait_scores(1, 1, 0, 0)
            scores(1, 0)
            lo_group(0, 0, 4)
            lo_group(0, 0, 5)
            wait_scores(1, 1, 0, 1)
            scores(1, 1)
            transpose_blocks(1, 0)
            lo_group(0, 0, 6)
            wait_scores(1, 1, 0, 2)
            scores(1, 2)
            transpose_blocks(1, 1)
            wait_scores(1, 1, 0, 3)
            scores(1, 3)
            lo_group(0, 0, 7)
            wait_scores(2, 0, 1, 0)
            scores(0, 0)
            lo_group(1, 1, 0)
            lo_group(1, 1, 1)
            wait_scores(2, 0, 1, 1)
            scores(0, 1)
            invert_sums(0, 0)
            lo_shuffle(1, 1, 0)
            lo_group(1, 1, 2)
            lo_group(1, 1, 3)
            for t in (2, 3):
                step(t, t - 2, 1)
            with dve.Fori(2, TILES // 2 - 1) as p:
                for u in range(2):
                    step(2 * p + u, u, p)
            for u in range(2):
                step(TILES - 2 + u, u, TILES // 2 - 1, more=(u == 0))
            lo_u(TILES - 2, 0)
            lo_shuffle(TILES - 1, 1, 1)
            invert_sums(TILES - 1, 1)
            lo_u(TILES - 2, 1)
            output(TILES - 2, 0, TILES // 2 - 1)
            lo_u(TILES - 1, 0)
            lo_u(TILES - 1, 1)
            output(TILES - 1, 1, TILES // 2 - 1)


_INS = ['x', 'adj', 'L0_gnn_W', 'L0_gnn_a']


def kernel(**inputs):
    import numpy as _np
    import concourse.bacc as _bacc
    from concourse import mybir as _mybir
    from concourse.bass_utils import run_bass_kernel_spmd as _run

    nc = _bacc.Bacc("TRN2", target_bir_lowering=False, num_devices=1)
    arrays, args = {}, []
    for name in _INS:
        arr = _np.ascontiguousarray(inputs[name])
        arrays[f"in_{name}_dram"] = arr
        args.append(nc.dram_tensor(f"in_{name}_dram", arr.shape, _mybir.dt.from_np(arr.dtype), kind="ExternalInput").ap())
    out = nc.dram_tensor("out_dram", inputs['x'].shape, _mybir.dt.float32, kind="ExternalOutput").ap()
    gat_layer(nc, *args, out)
    r = _run(nc, [arrays], core_ids=[0])
    return r.results[0]["out_dram"]
```
